# Optimizing a Trainium2 kernel written in Bass

```python
import numpy as np
import jax
import jax.numpy as jnp

def _softmax(x, axis=-1):
    return jax.nn.softmax(x, axis=axis)

def _gelu(x):
    return jax.nn.gelu(x, approximate=True)

def _silu(x):
    return jax.nn.silu(x)

def _sigmoid(x):
    return jax.nn.sigmoid(x)

def _layernorm(x, axis=-1, eps=1e-05):
    m = jnp.mean(x, axis=axis, keepdims=True)
    v = jnp.var(x, axis=axis, keepdims=True)
    return (x - m) / jnp.sqrt(v + eps)

def _scatter_add(tgt, idx, src, axis=0):
    return tgt.at[idx].add(src)

def _segment_sum(src, seg, n):
    return jax.ops.segment_sum(src, seg, n)
kernel_name = 'mk_cond_resid_d1_seqx_r4_b29770'

def setup_inputs(seed: int=0):
    np.random.seed(seed)
    _w = jnp.asarray

    def _rec_inputs():
        import jax
        import jax.numpy as jnp
        _rk = jax.random.key(seed)
        x = -0.000125 + 0.9999 * jax.random.normal(jax.random.fold_in(_rk, 1), (8, 256, 256), jnp.float32)
        _lenS = 256 - jax.random.randint(jax.random.fold_in(_rk, 7), (8,), 0, max(1, 256 // 4) + 1, jnp.int32)
        _lenS2 = 256 - jax.random.randint(jax.random.fold_in(_rk, 8), (8,), 0, max(1, 256 // 4) + 1, jnp.int32)
        cond_1024 = -0.00493535 + 1.00056 * jax.random.normal(jax.random.fold_in(_rk, 11), (8, 256), jnp.float32)
        return (x, cond_1024)
    x, cond_1024 = _rec_inputs()

    def _L0_cond_setup():
        import jax, jax.numpy as jnp
        import numpy as np

        def _lstm(x, h0, Wx, Wh, b):
            H = h0.shape[1]
            xW = jnp.einsum('ntd,dk->ntk', x, Wx) + b
            c0 = jnp.zeros_like(h0)

            def step(carry, xw_t):
                prev_h, prev_c = carry
                a = xw_t + prev_h @ Wh
                i = jax.nn.sigmoid(a[:, :H])
                f = jax.nn.sigmoid(a[:, H:2 * H])
                o = jax.nn.sigmoid(a[:, 2 * H:3 * H])
                g = jnp.tanh(a[:, 3 * H:])
                next_c = f * prev_c + i * g
                next_h = o * jnp.tanh(next_c)
                return ((next_h, next_c), next_h)
            _, hs = jax.lax.scan(step, (h0, c0), jnp.swapaxes(xW, 0, 1))
            return jnp.swapaxes(hs, 0, 1)
        key = jax.random.key(seed)
        k_x, k_h0, k_wx, k_wh = jax.random.split(key, 4)
        N, T, D, H = (64, 128, 256, 256)
        x = jax.random.normal(k_x, (N, T, D), dtype=jnp.float32)
        h0 = jax.random.normal(k_h0, (N, H), dtype=jnp.float32)
        Wx = jax.random.normal(k_wx, (D, 4 * H), dtype=jnp.float32) / jnp.sqrt(jnp.float32(D))
        Wh = jax.random.normal(k_wh, (H, 4 * H), dtype=jnp.float32) / jnp.sqrt(jnp.float32(H))
        b = jnp.zeros((4 * H,), dtype=jnp.float32)
        return {'x': x, 'h0': h0, 'Wx': Wx, 'Wh': Wh, 'b': b}
    _L0_cond_all = _L0_cond_setup()
    _L0_cond_in = {k: v for k, v in _L0_cond_all.items() if k in ('Wx', 'Wh', 'b')}
    del _L0_cond_all
    return {'x': x, 'cond_1024': cond_1024, 'L0_cond_Wx': _L0_cond_in['Wx'], 'L0_cond_Wh': _L0_cond_in['Wh'], 'L0_cond_b': _L0_cond_in['b']}

def reference(x, cond_1024, L0_cond_Wx, L0_cond_Wh, L0_cond_b):
    import jax
    import jax.numpy as jnp

    def _L0_cond_ref(x, h0, Wx, Wh, b):
        import jax, jax.numpy as jnp
        import numpy as np

        def _lstm(x, h0, Wx, Wh, b):
            H = h0.shape[1]
            xW = jnp.einsum('ntd,dk->ntk', x, Wx) + b
            c0 = jnp.zeros_like(h0)

            def step(carry, xw_t):
                prev_h, prev_c = carry
                a = xw_t + prev_h @ Wh
                i = jax.nn.sigmoid(a[:, :H])
                f = jax.nn.sigmoid(a[:, H:2 * H])
                o = jax.nn.sigmoid(a[:, 2 * H:3 * H])
                g = jnp.tanh(a[:, 3 * H:])
                next_c = f * prev_c + i * g
                next_h = o * jnp.tanh(next_c)
                return ((next_h, next_c), next_h)
            _, hs = jax.lax.scan(step, (h0, c0), jnp.swapaxes(xW, 0, 1))
            return jnp.swapaxes(hs, 0, 1)
        return _lstm(x, h0, Wx, Wh, b)
    x = x + _L0_cond_ref(x, cond_1024, L0_cond_Wx, L0_cond_Wh, L0_cond_b)
    return x

_drawn_inputs = setup_inputs


def setup_inputs(seed=0):
    import zlib

    import numpy as np

    out = dict(_drawn_inputs(seed))
    spreads = {'L0_cond_b': (0.0, 0.1)}
    factors = {'cond_1024': 4.727}
    for name, (base, spread) in spreads.items():
        noise = np.random.default_rng([zlib.crc32(name.encode()), seed]).standard_normal(out[name].shape)
        drawn = base * np.exp(spread * noise) if base else spread * noise
        out[name] = jnp.asarray(drawn.astype(out[name].dtype))
    for name, factor in factors.items():
        out[name] = (out[name] * factor).astype(out[name].dtype)
    return out
```

```python
from contextlib import ExitStack

import concourse.bass as bass
from concourse import mybir

F32 = mybir.dt.float32
ALU = mybir.AluOpType
ACT = mybir.ActivationFunctionType



def lstm_residual_kernel(nc, x, cond, Wx, Wh, b, out):
    N, T, D = x.shape
    HID = cond.shape[1]
    P = 128
    NG = 4
    QUAD = 32
    NQ = P // QUAD
    KC = HID // P
    BLOCK = 8
    NBLK = T // BLOCK
    ROWS = N * BLOCK
    COLS = KC * QUAD
    HALF = NG // 2
    PAD = QUAD - N
    STATE = NG * N
    assert D == HID and KC == 2 and N * NG == QUAD and HALF * ROWS == P

    x_blocks = x.rearrange("n (k t) d -> k n t d", t=BLOCK)
    out_blocks = out.rearrange("n (k t) d -> k n t d", t=BLOCK)

    with ExitStack() as ctx:
        def sb(name, shape, dt=F32):
            return ctx.enter_context(nc.sbuf_tensor(name, shape, dt))

        def pb(name, shape):
            return ctx.enter_context(nc.psum_tensor(name, shape, F32))

        def sem(name):
            return ctx.enter_context(nc.semaphore(name))

        wx_in = sb("wx_in", [P, KC, NG * HID])
        wh_in = sb("wh_in", [P, KC, NG * HID])
        wx = sb("wx", [P, KC, NG, HID])
        wh = sb("wh", [P, KC, NG, HID])
        b_in = sb("b_in", [1, NG * HID])
        bias = sb("bias", [1, NG, HID])
        ones = sb("ones", [1, ROWS])
        ident = sb("ident", [P, P])
        pick = sb("pick", [P, BLOCK, HALF, QUAD])
        cond_rows = sb("cond_rows", [N, HID])
        x_rows = sb("x_rows", [ROWS, D])
        x_res = sb("x_res", [ROWS, D])
        xT = sb("xT", [P, KC, ROWS])
        xproj = sb("xproj", [P, HALF, HID])
        hist = sb("hist", [P, KC, PAD + BLOCK * QUAD])
        gates = sb("gates", [P, COLS])
        gT = sb("gT", [P, 2, KC, STATE + N])
        ig_fc = sb("ig_fc", [P, KC, 2 * N])
        tanh_c = sb("tanh_c", [P, KC, N])
        h_dense = sb("h_dense", [P, KC, ROWS])
        y_rows = sb("y_rows", [ROWS, HID])

        gates_ps = [pb(f"gates_ps{k}", [P, 512]) for k in range(2)]
        proj_ps = [pb(f"proj_ps{k}", [P, 512]) for k in range(HALF)]
        xT_ps = pb("xT_ps", [P, 512])
        y_ps = pb("y_ps", [P, 512])

        wx_loaded = sem("wx_loaded")
        wh_loaded = sem("wh_loaded")
        small_loaded = sem("small_loaded")
        x_loaded = sem("x_loaded")
        res_loaded = sem("res_loaded")
        y_stored = sem("y_stored")
        zeros_set = sem("zeros_set")
        ident_set = sem("ident_set")
        pick_set = sem("pick_set")
        wx_scaled = sem("wx_scaled")
        wh_scaled = sem("wh_scaled")
        bias_scaled = sem("bias_scaled")
        cond_turned = sem("cond_turned")
        x_turned = sem("x_turned")
        xT_ready = sem("xT_ready")
        proj_done = sem("proj_done")
        proj_copied0 = sem("proj_copied0")
        proj_copied1 = sem("proj_copied1")
        injected = sem("injected")
        gates_done = sem("gates_done")
        tanh_done = sem("tanh_done")
        dve_link = sem("dve_link")
        c_ready = sem("c_ready")
        tanh_c_ready = sem("tanh_c_ready")
        h_ready = sem("h_ready")
        h_packed = sem("h_packed")
        y_turned = sem("y_turned")
        y_ready = sem("y_ready")

        def window(c, slot, q):
            at = PAD + QUAD * slot - N * q
            return hist[:, c, at:at + QUAD]

        def hslot(slot):
            return hist[:, :, PAD + QUAD * slot:PAD + QUAD * slot + N]

        block = ctx.enter_context(nc.Block())

        @block.sync
        def _(sp):
            def load_x(k):
                sp.dma_start(x_rows[:, :], x_blocks[k]).then_inc(x_loaded, 16)

            def load_res(k):
                sp.dma_start(x_res[:, :], x_blocks[k]).then_inc(res_loaded, 16)

            def store_y(k):
                sp.wait_ge(y_ready, k + 1)
                sp.dma_start(out_blocks[k], y_rows[:, :]).then_inc(y_stored, 16)

            load_x(0)
            sp.dma_start(cond_rows[:, :], cond).then_inc(small_loaded, 16)
            sp.dma_start(b_in[:, :], b.rearrange("(a k) -> a k", a=1)).then_inc(small_loaded, 16)
            sp.dma_start(wx_in[:, :, :], Wx.rearrange("(c p) k -> p c k", p=P)).then_inc(wx_loaded, 16)
            load_res(0)
            sp.wait_ge(x_turned, 1)
            load_x(1)
            with sp.Fori(1, NBLK - 1) as k:
                sp.wait_ge(x_turned, k + 1)
                load_x(k + 1)
                store_y(k - 1)
                sp.wait_ge(y_stored, 16 * k)
                load_res(k)
            store_y(NBLK - 2)
            sp.wait_ge(y_stored, 16 * (NBLK - 1))
            load_res(NBLK - 1)
            store_y(NBLK - 1)
            sp.wait_ge(y_stored, 16 * NBLK)

        @block.gpsimd
        def _(pool):
            nc.gpsimd.memset(ident[:, :], 0.0).then_inc(ident_set, 1)
            pool.wait_ge(ident_set, 1)
            nc.gpsimd.affine_select(out=ident[:, :], in_=ident[:, :], compare_op=ALU.not_equal, fill=1.0,
                                    base=0, pattern=[[-1, P]], channel_multiplier=1).then_inc(ident_set, 1)
            nc.gpsimd.memset(pick[:, :, :, :], 0.0).then_inc(pick_set, 1)
            pool.wait_ge(ident_set, 2)
            pool.wait_ge(pick_set, 1)
            for hi in range(HALF):
                rows = ident[:, ROWS * hi:ROWS * (hi + 1)].rearrange("p (n t) -> p t n", n=N)
                for e in range(HALF):
                    q = HALF * hi + e
                    nc.gpsimd.tensor_copy(pick[:, :, e, N * q:N * (q + 1)], rows).then_inc(pick_set, 1)

        @block.scalar
        def _(act):
            act.dma_start(wh_in[:, :, :], Wh.rearrange("(c p) k -> p c k", p=P)).then_inc(wh_loaded, 16)

            def copy_proj(k):
                act.wait_ge(proj_done, k + 1)
                act.wait_ge(injected, BLOCK * k)
                nc.scalar.copy(xproj[:, 0, :], proj_ps[0][:, 0:HID]).then_inc(proj_copied0, 1)

            def pack_h(k):
                act.wait_ge(h_ready, BLOCK * (k + 1) + 1)
                nc.scalar.copy(h_dense[:, :, :].rearrange("p c (n t) -> p c n t", n=N),
                               hist[:, :, PAD:PAD + BLOCK * QUAD].rearrange("p c (t m) -> p c m t", m=QUAD)[:, :, 0:N, :]
                               ).then_inc(h_packed, 1)

            def step(k, s):
                t = BLOCK * k + s
                act.wait_ge(gates_done, t + 1)
                nc.scalar.activation(gates[:, :], gates_ps[s % 2][:, 0:COLS], ACT.Tanh).then_inc(tanh_done, 1)
                act.wait_ge(c_ready, t + 1)
                nc.scalar.activation(tanh_c[:, :, :], gT[:, (s + 1) % 2, :, STATE:STATE + N], ACT.Tanh,
                                     scale=0.5).then_inc(tanh_c_ready, 1)

            def steps(k, first=False, last=False):
                for s in range(BLOCK):
                    if s == 0 and not first:
                        pack_h(k - 1)
                    if s == BLOCK - 1 and not last:
                        copy_proj(k + 1)
                    step(k, s)

            def scale(w_out, w_in, c, q, factor, done):
                return nc.scalar.mul(w_out[:, c, q, :].rearrange("p (g c u) -> p g c u", g=NQ, c=KC),
                                     w_in[:, c, q * HID:(q + 1) * HID].rearrange("p (c g u) -> p g c u", g=NQ, c=KC),
                                     factor).then_inc(done, 1)

            act.wait_ge(wx_loaded, 16)
            for q in range(NG):
                scale(wx, wx_in, 1, q, 0.5 if q < NG - 1 else 1.0, wx_scaled)
            act.wait_ge(wh_loaded, 16)
            for q in range(NG):
                scale(wh, wh_in, 1, q, 0.25 if q < NG - 1 else 0.5, wh_scaled)
            act.wait_ge(proj_done, 1)
            nc.scalar.copy(xproj[:, 0, :], proj_ps[0][:, 0:HID]).then_inc(proj_copied0, 1)
            steps(0, first=True)
            with act.Fori(1, NBLK - 1) as k:
                steps(k)
            steps(NBLK - 1, last=True)
            pack_h(NBLK - 1)

        @block.vector
        def _(dve):
            def copy_xT(k):
                dve.wait_ge(x_turned, k + 1)
                nc.vector.tensor_copy(xT[:, :, :], xT_ps[:, 0:KC * ROWS].rearrange("p (c r) -> p c r", c=KC)).then_inc(xT_ready, 1)

            def copy_proj(k):
                dve.wait_ge(proj_done, k + 1)
                dve.wait_ge(injected, BLOCK * k)
                nc.vector.tensor_copy(xproj[:, 1, :], proj_ps[1][:, 0:HID]).then_inc(proj_copied1, 1)

            def add_x(k):
                dve.wait_ge(y_turned, k + 1)
                dve.wait_ge(res_loaded, 16 * (k + 1))
                nc.vector.scalar_tensor_tensor(out=y_rows[:, :], in0=y_ps[0:ROWS, 0:HID], scalar=0.5, in1=x_res[:, :],
                                               op0=ALU.mult, op1=ALU.add).then_inc(y_ready, 1)

            def step(k, s, store):
                t = BLOCK * k + s
                g = gT[:, s % 2, :, :]
                c_next = gT[:, (s + 1) % 2, :, STATE:STATE + N]
                dve.wait_ge(tanh_done, t + 1)
                nc.vector.transpose(g[:, :, 0:STATE], gates[:, :].rearrange("p (c u) -> p c u", c=KC)).then_inc(dve_link, 1)
                dve.wait_ge(dve_link, 2 * t + 1)
                nc.vector.scalar_tensor_tensor(out=ig_fc[:, :, :], in0=g[:, :, 0:2 * N], scalar=1.0,
                                               in1=g[:, :, 3 * N:5 * N], op0=ALU.add, op1=ALU.mult).then_inc(dve_link, 1)
                dve.wait_ge(dve_link, 2 * t + 2)
                nc.vector.scalar_tensor_tensor(out=c_next, in0=ig_fc[:, :, N:2 * N], scalar=0.5,
                                               in1=ig_fc[:, :, 0:N], op0=ALU.mult, op1=ALU.add).then_inc(c_ready, 1)
                if store and s == 0:
                    dve.wait_ge(h_packed, k)
                dve.wait_ge(tanh_c_ready, t + 1)
                nc.vector.scalar_tensor_tensor(out=hslot(s), in0=g[:, :, 2 * N:3 * N], scalar=1.0,
                                               in1=tanh_c[:, :, :], op0=ALU.add, op1=ALU.mult).then_inc(h_ready, 1)

            def steps(k, first=False, last=False):
                for s in range(BLOCK):
                    if s == 2 and not first:
                        add_x(k - 1)
                    if s == 1 and not last:
                        copy_xT(k + 1)
                    if s == BLOCK - 1 and not last:
                        copy_proj(k + 1)
                    step(k, s, store=not first)

            nc.vector.memset(hist[:, :, :], 0.0).then_inc(zeros_set, 1)
            nc.vector.memset(gT[:, 0, :, :], 0.0).then_inc(zeros_set, 1)
            nc.vector.memset(ones[:, :], 1.0).then_inc(zeros_set, 1)
            dve.wait_ge(small_loaded, 32)
            bias_v = bias[:, :, :].rearrange("p q (g c u) -> p q g c u", g=NQ, c=KC)
            b_v = b_in[:, :].rearrange("p (q c g u) -> p q g c u", q=NG, g=NQ, c=KC)
            for q in range(NG):
                nc.vector.tensor_scalar(bias_v[:, q], b_v[:, q], 0.5 if q < NG - 1 else 1.0, None,
                                        ALU.mult).then_inc(bias_scaled, 1)
            dve.wait_ge(zeros_set, 1)
            dve.wait_ge(cond_turned, 1)
            nc.vector.tensor_scalar(hslot(BLOCK - 1), y_ps[:, 0:KC * N].rearrange("p (c n) -> p c n", c=KC), 2.0, None,
                                    ALU.mult).then_inc(h_ready, 1)
            copy_xT(0)

            def scale(w_out, w_in, c, q, factor, done):
                nc.vector.tensor_scalar(w_out[:, c, q, :].rearrange("p (g c u) -> p g c u", g=NQ, c=KC),
                                        w_in[:, c, q * HID:(q + 1) * HID].rearrange("p (c g u) -> p g c u", g=NQ, c=KC),
                                        factor, None, ALU.mult).then_inc(done, 1)

            dve.wait_ge(wx_loaded, 16)
            for q in range(NG):
                scale(wx, wx_in, 0, q, 0.5 if q < NG - 1 else 1.0, wx_scaled)
            dve.wait_ge(wh_loaded, 16)
            for q in range(NG):
                scale(wh, wh_in, 0, q, 0.25 if q < NG - 1 else 0.5, wh_scaled)
            dve.wait_ge(proj_done, 1)
            nc.vector.tensor_copy(xproj[:, 1, :], proj_ps[1][:, 0:HID]).then_inc(proj_copied1, 1)
            dve.wait_ge(zeros_set, 3)
            steps(0, first=True)
            with dve.Fori(1, NBLK - 1) as k:
                steps(k)
            steps(NBLK - 1, last=True)
            add_x(NBLK - 1)

        @block.tensor
        def _(pe):
            def turn_x():
                for c in range(KC):
                    last = nc.tensor.transpose(xT_ps[:, c * ROWS:(c + 1) * ROWS], x_rows[:, c * P:(c + 1) * P],
                                               ident[0:ROWS, 0:ROWS])
                last.then_inc(x_turned, 1)

            PIECES = 2

            def project(piece):
                e, part = piece // PIECES, piece % PIECES
                w = HID // PIECES
                cols = slice(part * w, (part + 1) * w)
                for hi in range(HALF):
                    nc.tensor.matmul(proj_ps[e][ROWS * hi:ROWS * (hi + 1), cols], ones[:, :],
                                     bias[:, HALF * hi + e, cols], start=(part == 0), stop=False,
                                     skip_group_check=True)
                for c in range(KC):
                    for hi in range(HALF):
                        last = nc.tensor.matmul(proj_ps[e][ROWS * hi:ROWS * (hi + 1), cols], xT[:, c, :],
                                                wx[:, c, HALF * hi + e, cols], start=False,
                                                stop=(c == KC - 1), skip_group_check=True)
                if piece == HALF * PIECES - 1:
                    last.then_inc(proj_done, 1)

            def inject(s, par):
                for e in range(HALF):
                    for g in range(NQ):
                        last = nc.tensor.matmul(gates_ps[par][QUAD * g:QUAD * (g + 1), 0:COLS], pick[:, s, e, :],
                                                xproj[:, e, COLS * g:COLS * (g + 1)], start=(e == 0), stop=False,
                                                skip_group_check=True)
                last.then_inc(injected, 1)

            def recur(k, s):
                pe.wait_ge(h_ready, BLOCK * k + s + 1)
                for c in range(KC):
                    for q in range(NG):
                        for g in range(NQ):
                            last = nc.tensor.matmul(gates_ps[s % 2][QUAD * g:QUAD * (g + 1), 0:COLS],
                                                    window(c, (s - 1) % BLOCK, q),
                                                    wh[:, c, q, COLS * g:COLS * (g + 1)], start=False,
                                                    stop=(c == KC - 1 and q == NG - 1), skip_group_check=True)
                last.then_inc(gates_done, 1)

            def turn_y():
                for c in range(KC):
                    last = nc.tensor.transpose(y_ps[0:ROWS, c * P:(c + 1) * P], h_dense[:, c, :], ident[:, :])
                last.then_inc(y_turned, 1)

            def steps(k, first=False, last=False):
                for s in range(BLOCK):
                    recur(k, s)
                    if s == 0 and not last:
                        pe.wait_ge(x_loaded, 16 * (k + 2))
                    if s == 1 and not first:
                        pe.wait_ge(h_packed, k)
                    if s < BLOCK - 1:
                        inject(s + 1, (s + 1) % 2)
                    elif not last:
                        pe.wait_ge(proj_copied0, k + 2)
                        pe.wait_ge(proj_copied1, k + 2)
                        inject(0, 0)
                    if s == 0 and not last:
                        turn_x()
                    if s == 1 and not first:
                        turn_y()
                    if 2 <= s < 2 + HALF * PIECES and not last:
                        if s == 2:
                            pe.wait_ge(xT_ready, k + 2)
                        project(s - 2)

            pe.wait_ge(ident_set, 2)
            pe.wait_ge(small_loaded, 32)
            for c in range(KC):
                last = nc.tensor.transpose(y_ps[:, c * N:(c + 1) * N], cond_rows[:, c * P:(c + 1) * P], ident[0:N, 0:N])
            last.then_inc(cond_turned, 1)
            pe.wait_ge(x_loaded, 16)
            turn_x()
            pe.wait_ge(zeros_set, 3)
            pe.wait_ge(bias_scaled, NG)
            pe.wait_ge(xT_ready, 1)
            pe.wait_ge(wx_scaled, KC * NG)
            for piece in range(HALF * PIECES):
                project(piece)
            pe.wait_ge(pick_set, 1 + HALF * HALF)
            pe.wait_ge(proj_copied0, 1)
            pe.wait_ge(proj_copied1, 1)
            inject(0, 0)
            pe.wait_ge(wh_scaled, KC * NG)
            steps(0, first=True)
            with pe.Fori(1, NBLK - 1) as k:
                steps(k)
            steps(NBLK - 1, last=True)
            pe.wait_ge(h_packed, NBLK)
            turn_y()


_INS = ['x', 'cond_1024', 'L0_cond_Wx', 'L0_cond_Wh', 'L0_cond_b']
_OUTS = [((8, 256, 256), 'float32')]


def kernel(**inputs):
    import numpy as _np
    import concourse.bacc as _bacc
    from concourse import mybir as _mybir
    from concourse.bass_utils import run_bass_kernel_spmd as _run

    nc = _bacc.Bacc("TRN2", target_bir_lowering=False, num_devices=1)
    arrays, args = {}, []
    for name in _INS:
        a = _np.ascontiguousarray(inputs[name])
        arrays[f"in_{name}_dram"] = a
        args.append(nc.dram_tensor(f"in_{name}_dram", a.shape, _mybir.dt.from_np(a.dtype), kind="ExternalInput").ap())
    for i, (shape, dtype) in enumerate(_OUTS):
        dt = _mybir.dt.from_np(_np.dtype(dtype))
        args.append(nc.dram_tensor(f"out_{i}_dram", shape, dt, kind="ExternalOutput").ap())
    lstm_residual_kernel(nc, *args)
    r = _run(nc, [arrays], core_ids=[0])
    got = tuple(r.results[0][f"out_{i}_dram"] for i in range(len(_OUTS)))
    return got[0]
```

```python
from contextlib import ExitStack

import concourse.bass as bass
from concourse import mybir

F32 = mybir.dt.float32
ALU = mybir.AluOpType
ACT = mybir.ActivationFunctionType



def lstm_residual_kernel(nc, x, cond, Wx, Wh, b, out):
    N, T, D = x.shape
    HID = cond.shape[1]
    P = 128
    NG = 4
    U = 32
    NQ = P // U
    NC = HID // P
    GW = NG * U
    BLOCK = 8
    NBLK = T // BLOCK
    ROWS = N * BLOCK
    assert D == HID and NC == 2 and NC * ROWS == P and T % BLOCK == 0

    x_blocks = x.rearrange("n (k t) d -> k n t d", t=BLOCK)
    x_quads = x.rearrange("n (k t) (g j) -> k g n t j", t=BLOCK, g=NQ)
    out_quads = out.rearrange("n (k t) (g j) -> k g n t j", t=BLOCK, g=NQ)

    with ExitStack() as ctx:
        def sb(name, shape, dt=F32):
            return ctx.enter_context(nc.sbuf_tensor(name, shape, dt))

        def pb(name):
            return ctx.enter_context(nc.psum_tensor(name, [P, 512], F32))

        def sem(name):
            return ctx.enter_context(nc.semaphore(name))

        wx_in = sb("wx_in", [P, NC, NG * HID])
        wh_in = sb("wh_in", [P, NC, NG * HID])
        wx = sb("wx", [P, NC, NQ, NC, GW])
        wh = sb("wh", [P, NC, NQ, NC, GW])
        b_all = sb("b_all", [P, NG * HID])
        bias = sb("bias", [P, 2, NC, GW])
        ident = sb("ident", [P, P])
        pick = sb("pick", [P, BLOCK, 2, N])
        x_rows = sb("x_rows", [ROWS, D])
        xT = sb("xT", [P, NC, ROWS])
        xproj = sb("xproj", [P, 2, NC, GW])
        h_rows = sb("h_rows", [P, BLOCK, NC, U])
        h0_rows = sb("h0_rows", [P, NC, U])
        hT = sb("hT", [P, NC, U])
        xy = sb("xy", [P, BLOCK, NC, U])
        gates = sb("gates", [P, 2, NC, GW + U])
        products = sb("products", [P, NC, 2 * U])
        tanh_c = sb("tanh_c", [P, NC, U])

        gates_ps = [[pb(f"gates_ps{k}{c}") for c in range(NC)] for k in range(2)]
        proj_ps = pb("proj_ps")
        xT_ps = pb("xT_ps")

        wx_loaded = sem("wx_loaded")
        wh_loaded = sem("wh_loaded")
        b_loaded = sem("b_loaded")
        h0_loaded = sem("h0_loaded")
        x_loaded = sem("x_loaded")
        xy_loaded = sem("xy_loaded")
        y_stored = sem("y_stored")
        zeros_set = sem("zeros_set")
        ps_zeroed = sem("ps_zeroed")
        ident_set = sem("ident_set")
        pick_set = sem("pick_set")
        wx_scaled = sem("wx_scaled")
        wh_scaled = sem("wh_scaled")
        bias_set = sem("bias_set")
        h0_scaled = sem("h0_scaled")
        x_turned = sem("x_turned")
        xT_ready = sem("xT_ready")
        proj_done = sem("proj_done")
        proj_ready = sem("proj_ready")
        injected = sem("injected")
        gates_done = [sem(f"gates_done{c}") for c in range(NC)]
        tanh_done = [sem(f"tanh_done{c}") for c in range(NC)]
        products_done = [sem(f"products_done{c}") for c in range(NC)]
        c_ready = [sem(f"c_ready{c}") for c in range(NC)]
        tanh_c_done = [sem(f"tanh_c_done{c}") for c in range(NC)]
        h_rows_done = [sem(f"h_rows_done{c}") for c in range(NC)]
        hT_ready = [sem(f"hT_ready{c}") for c in range(NC)]
        y_ready = sem("y_ready")

        block = ctx.enter_context(nc.Block())

        @block.sync
        def _(sp):
            def load_x(k):
                sp.dma_start(x_rows[:, :], x_blocks[k]).then_inc(x_loaded, 16)

            def load_xy(k):
                for g in range(NQ):
                    sp.dma_start(xy[U * g:U * g + N, :, :, :].rearrange("p t c u -> p t (c u)"),
                                 x_quads[k, g]).then_inc(xy_loaded, 16)

            def store_y(k):
                sp.wait_ge(y_ready, 2 * k + 2)
                for g in range(NQ):
                    sp.dma_start(out_quads[k, g],
                                 xy[U * g:U * g + N, :, :, :].rearrange("p t c u -> p t (c u)")).then_inc(y_stored, 16)

            load_x(0)
            sp.dma_start(wx_in[:, :, :], Wx.rearrange("(c p) k -> p c k", p=P)).then_inc(wx_loaded, 16)
            sp.dma_start(b_all[:, :], b.partition_broadcast(P)).then_inc(b_loaded, 16)
            sp.wait_ge(zeros_set, 3)
            for g in range(NQ):
                sp.dma_start(h0_rows[U * g:U * g + N, :, :].rearrange("p c u -> p (c u)"),
                             cond[:, 2 * U * g:2 * U * (g + 1)]).then_inc(h0_loaded, 16)
            load_xy(0)
            sp.wait_ge(x_turned, 1)
            load_x(1)

            def swap_xy(k):
                store_y(k)
                sp.wait_ge(y_stored, 16 * NQ * (k + 1))
                load_xy(k + 1)

            with sp.Fori(0, NBLK - 2) as k:
                sp.wait_ge(x_turned, k + 2)
                load_x(k + 2)
                swap_xy(k)
            swap_xy(NBLK - 2)
            store_y(NBLK - 1)
            sp.wait_ge(y_stored, 16 * NQ * NBLK)

        @block.gpsimd
        def _(pool):
            nc.gpsimd.memset(ident[:, :], 0.0).then_inc(ident_set, 1)
            pool.wait_ge(ident_set, 1)
            nc.gpsimd.affine_select(out=ident[:, :], in_=ident[:, :], compare_op=ALU.not_equal, fill=1.0,
                                    base=0, pattern=[[-1, P]], channel_multiplier=1).then_inc(ident_set, 1)
            pool.wait_ge(ident_set, 2)
            for hi in range(2):
                nc.gpsimd.tensor_copy(pick[:, :, hi, :],
                                      ident[:, ROWS * hi:ROWS * (hi + 1)].rearrange("p (n t) -> p t n", n=N)
                                      ).then_inc(pick_set, 1)

        def scaled(w_out, w_in, c, q):
            return (w_out[:, c, :, :, U * q:U * (q + 1)],
                    w_in[:, c, HID * q:HID * (q + 1)].rearrange("p (g c u) -> p g c u", g=NQ, c=NC))

        WX_SCALE = [0.5, 0.5, 0.5, 1.0]
        WH_SCALE = [0.25, 0.25, 0.25, 0.5]

        @block.scalar
        def _(act):
            for g in range(NQ):
                act.dma_start(wh_in[U * g:U * (g + 1), :, :],
                              Wh[2 * U * g:2 * U * (g + 1), :].rearrange("(c u) k -> u c k", c=NC)).then_inc(wh_loaded, 16)
            act.wait_ge(wx_loaded, 16)
            for q in range(NG):
                nc.scalar.mul(*scaled(wx, wx_in, 1, q), WX_SCALE[q]).then_inc(wx_scaled, 1)
            act.wait_ge(wh_loaded, 16 * NQ)
            for q in range(NG):
                nc.scalar.mul(*scaled(wh, wh_in, 1, q), WH_SCALE[q]).then_inc(wh_scaled, 1)

            def step(k, s):
                t = BLOCK * k + s
                for c in range(NC):
                    act.wait_ge(gates_done[c], t + 1)
                    nc.scalar.activation(gates[:, s % 2, c, 0:GW], gates_ps[s % 2][c][:, 0:GW],
                                         ACT.Tanh).then_inc(tanh_done[c], 1)
                for c in range(NC):
                    act.wait_ge(c_ready[c], t + 1)
                    nc.scalar.activation(tanh_c[:, c, :], gates[:, (s + 1) % 2, c, GW:GW + U], ACT.Tanh,
                                         scale=0.5).then_inc(tanh_c_done[c], 1)

            with act.Fori(0, NBLK) as k:
                for s in range(BLOCK):
                    step(k, s)

        @block.vector
        def _(dve):
            def copy_xT(k):
                dve.wait_ge(x_turned, k + 1)
                nc.vector.tensor_copy(xT[:, :, :], xT_ps[:, 0:NC * ROWS].rearrange("p (c r) -> p c r", c=NC)
                                      ).then_inc(xT_ready, 1)

            def copy_proj(k, gg):
                cols = slice(NC * GW * gg, NC * GW * (gg + 1))
                nc.vector.tensor_tensor(xproj[:, gg, :, :].rearrange("p c w -> p (c w)"), proj_ps[:, cols],
                                        bias[:, gg, :, :].rearrange("p c w -> p (c w)"), ALU.add).then_inc(proj_ready, 1)

            def add_x(k, part):
                steps_of = slice(BLOCK // 2 * part, BLOCK // 2 * (part + 1))
                xv = xy[:, steps_of, :, :].rearrange("p t c u -> p (t c u)")
                nc.vector.scalar_tensor_tensor(out=xv, in0=h_rows[:, steps_of, :, :].rearrange("p t c u -> p (t c u)"),
                                               scalar=0.5, in1=xv, op0=ALU.mult, op1=ALU.add).then_inc(y_ready, 1)

            def state(k, s, c):
                t = BLOCK * k + s
                G = gates[:, s % 2, c, :]
                dve.wait_ge(tanh_done[c], t + 1)
                nc.vector.scalar_tensor_tensor(out=products[:, c, :], in0=G[:, 0:2 * U], scalar=1.0,
                                               in1=G[:, 3 * U:5 * U], op0=ALU.add, op1=ALU.mult).then_inc(products_done[c], 1)
                dve.wait_ge(products_done[c], t + 1)
                nc.vector.scalar_tensor_tensor(out=gates[:, (s + 1) % 2, c, GW:GW + U], in0=products[:, c, U:2 * U],
                                               scalar=0.5, in1=products[:, c, 0:U], op0=ALU.mult,
                                               op1=ALU.add).then_inc(c_ready[c], 1)

            def hidden(k, s, c):
                t = BLOCK * k + s
                dve.wait_ge(tanh_c_done[c], t + 1)
                nc.vector.scalar_tensor_tensor(out=h_rows[:, s, c, :], in0=gates[:, s % 2, c, 2 * U:3 * U], scalar=1.0,
                                               in1=tanh_c[:, c, :], op0=ALU.add, op1=ALU.mult).then_inc(h_rows_done[c], 1)
                dve.wait_ge(h_rows_done[c], t + 1)
                nc.vector.transpose(hT[:, c, :], h_rows[:, s, c, :]).then_inc(hT_ready[c], 1)

            def steps(k, last=False):
                for s in range(BLOCK):
                    for c in range(NC):
                        state(k, s, c)
                    for c in range(NC):
                        hidden(k, s, c)
                    if s == 1 and not last:
                        copy_xT(k + 1)
                    if s == BLOCK // 2:
                        dve.wait_ge(xy_loaded, 16 * NQ * (k + 1))
                        add_x(k, 0)
                    if s == BLOCK - 2 and not last:
                        dve.wait_ge(proj_done, k + 2)
                        dve.wait_ge(injected, BLOCK * (k + 1))
                        copy_proj(k + 1, 0)
                        copy_proj(k + 1, 1)
                    if s == BLOCK - 1:
                        dve.wait_ge(h_rows_done[1], BLOCK * (k + 1))
                        add_x(k, 1)

            nc.vector.memset(h0_rows[:, :, :], 0.0).then_inc(zeros_set, 1)
            nc.vector.memset(xy[:, :, :, :], 0.0).then_inc(zeros_set, 1)
            nc.vector.memset(gates[:, 0, :, GW:GW + U], 0.0).then_inc(zeros_set, 1)
            for k in range(2):
                for c in range(NC):
                    nc.vector.memset(gates_ps[k][c][:, :], 0.0).then_inc(ps_zeroed, 1)
            dve.wait_ge(x_turned, 1)
            copy_xT(0)
            dve.wait_ge(b_loaded, 16)
            for hi in range(2):
                part = slice(ROWS * hi, ROWS * (hi + 1))
                for q in range(NG):
                    at = HID * q + 4 * U * hi
                    nc.vector.tensor_scalar(bias[part, :, :, U * q:U * (q + 1)],
                                            b_all[part, at:at + 4 * U].rearrange("p (g c u) -> p g c u", g=2, c=NC),
                                            WX_SCALE[q], None, ALU.mult).then_inc(bias_set, 1)
            dve.wait_ge(h0_loaded, 16 * NQ)
            nc.vector.tensor_scalar(h0_rows[:, :, :], h0_rows[:, :, :], 2.0, None, ALU.mult).then_inc(h0_scaled, 1)
            dve.wait_ge(h0_scaled, 1)
            for c in range(NC):
                nc.vector.transpose(hT[:, c, :], h0_rows[:, c, :]).then_inc(hT_ready[c], 1)
            dve.wait_ge(wx_loaded, 16)
            for q in range(NG):
                nc.vector.tensor_scalar(*scaled(wx, wx_in, 0, q), WX_SCALE[q], None, ALU.mult).then_inc(wx_scaled, 1)
            dve.wait_ge(wh_loaded, 16 * NQ)
            for q in range(NG):
                nc.vector.tensor_scalar(*scaled(wh, wh_in, 0, q), WH_SCALE[q], None, ALU.mult).then_inc(wh_scaled, 1)
            dve.wait_ge(bias_set, 2 * NG)
            dve.wait_ge(proj_done, 1)
            copy_proj(0, 0)
            copy_proj(0, 1)
            dve.wait_ge(zeros_set, 3)
            with dve.Fori(0, NBLK - 1) as k:
                steps(k)
            steps(NBLK - 1, last=True)

        @block.tensor
        def _(pe):
            def turn_x():
                for c in range(NC):
                    last = nc.tensor.transpose(xT_ps[:, c * ROWS:(c + 1) * ROWS], x_rows[:, c * P:(c + 1) * P],
                                               ident[0:ROWS, 0:ROWS])
                last.then_inc(x_turned, 1)

            def project(gg, co):
                cols = slice(GW * (NC * gg + co), GW * (NC * gg + co + 1))
                for c in range(NC):
                    for hi in range(2):
                        last = nc.tensor.matmul(proj_ps[ROWS * hi:ROWS * (hi + 1), cols], xT[:, c, :],
                                                wx[:, c, 2 * hi + gg, co, :], start=(c == 0 and gg == 0 and co == 0),
                                                stop=(c == NC - 1), skip_group_check=True)
                if gg == 1 and co == NC - 1:
                    last.then_inc(proj_done, 1)

            def inject(s):
                for co in range(NC):
                    for g in range(NQ):
                        last = nc.tensor.matmul(gates_ps[s % 2][co][U * g:U * g + N, 0:GW], pick[:, s, g // 2, :],
                                                xproj[:, g % 2, co, :], start=True, stop=False,
                                                skip_group_check=True)
                last.then_inc(injected, 1)

            def recur(s, c, co):
                for g in range(NQ):
                    last = nc.tensor.matmul(gates_ps[s % 2][co][U * g:U * g + N, 0:GW], hT[:, c, 0:N],
                                            wh[:, c, g, co, :], start=False, stop=(c == NC - 1),
                                            skip_group_check=True)
                return last

            def steps(k, last=False):
                for s in range(BLOCK):
                    t = BLOCK * k + s
                    pe.wait_ge(hT_ready[0], t + 1)
                    recur(s, 0, 0)
                    recur(s, 0, 1)
                    pe.wait_ge(hT_ready[1], t + 1)
                    recur(s, 1, 0).then_inc(gates_done[0], 1)
                    recur(s, 1, 1).then_inc(gates_done[1], 1)
                    if s == 0 and not last:
                        pe.wait_ge(x_loaded, 16 * (k + 2))
                    if s == 2 and not last:
                        pe.wait_ge(xT_ready, k + 2)
                    if s < BLOCK - 1:
                        inject(s + 1)
                    elif not last:
                        pe.wait_ge(proj_ready, 2 * (k + 2))
                        inject(0)
                    if s == 0 and not last:
                        turn_x()
                    if 2 <= s < 6 and not last:
                        project((s - 2) // 2, (s - 2) % 2)

            pe.wait_ge(ident_set, 2)
            pe.wait_ge(x_loaded, 16)
            turn_x()
            pe.wait_ge(xT_ready, 1)
            pe.wait_ge(wx_scaled, NC * NG)
            for gg in range(2):
                for co in range(NC):
                    project(gg, co)
            pe.wait_ge(pick_set, 2)
            pe.wait_ge(ps_zeroed, 2 * NC)
            pe.wait_ge(proj_ready, 2)
            inject(0)
            pe.wait_ge(wh_scaled, NC * NG)
            with pe.Fori(0, NBLK - 1) as k:
                steps(k)
            steps(NBLK - 1, last=True)


_INS = ['x', 'cond_1024', 'L0_cond_Wx', 'L0_cond_Wh', 'L0_cond_b']
_OUTS = [((8, 256, 256), 'float32')]


def kernel(**inputs):
    import numpy as _np
    import concourse.bacc as _bacc
    from concourse import mybir as _mybir
    from concourse.bass_utils import run_bass_kernel_spmd as _run

    nc = _bacc.Bacc("TRN2", target_bir_lowering=False, num_devices=1)
    arrays, args = {}, []
    for name in _INS:
        a = _np.ascontiguousarray(inputs[name])
        arrays[f"in_{name}_dram"] = a
        args.append(nc.dram_tensor(f"in_{name}_dram", a.shape, _mybir.dt.from_np(a.dtype), kind="ExternalInput").ap())
    for i, (shape, dtype) in enumerate(_OUTS):
        dt = _mybir.dt.from_np(_np.dtype(dtype))
        args.append(nc.dram_tensor(f"out_{i}_dram", shape, dt, kind="ExternalOutput").ap())
    lstm_residual_kernel(nc, *args)
    r = _run(nc, [arrays], core_ids=[0])
    got = tuple(r.results[0][f"out_{i}_dram"] for i in range(len(_OUTS)))
    return got[0]
```

```python
from contextlib import ExitStack

import concourse.bass as bass
from concourse import mybir

F32 = mybir.dt.float32
ALU = mybir.AluOpType
ACT = mybir.ActivationFunctionType



def lstm_residual_kernel(nc, x, cond, Wx, Wh, b, out):
    N, T, D = x.shape
    HID = cond.shape[1]
    P = 128
    NG = 4
    U = 32
    NQ = P // U
    NC = HID // P
    COLS = NG * NC * U
    IFG = 3 * U
    PARTS = [slice(0, IFG), slice(IFG, 2 * IFG), slice(2 * IFG, COLS)]
    GATE_AT = [0, U, 2 * IFG, 2 * U]
    GATE_STEP = [IFG, IFG, U, IFG]
    BLOCK = 8
    NBLK = T // BLOCK
    ROWS = N * BLOCK
    assert D == HID and NC == 2 and NC * ROWS == P and T % BLOCK == 0

    x_blocks = x.rearrange("n (k t) d -> k n t d", t=BLOCK)
    x_quads = x.rearrange("n (k t) (g j) -> k g n t j", t=BLOCK, g=NQ)
    out_quads = out.rearrange("n (k t) (g j) -> k g n t j", t=BLOCK, g=NQ)

    with ExitStack() as ctx:
        def sb(name, shape, dt=F32):
            return ctx.enter_context(nc.sbuf_tensor(name, shape, dt))

        def pb(name):
            return ctx.enter_context(nc.psum_tensor(name, [P, 512], F32))

        def sem(name):
            return ctx.enter_context(nc.semaphore(name))

        wx_in = sb("wx_in", [P, NC, NG * HID])
        wh_in = sb("wh_in", [P, NC, NG * HID])
        wx = sb("wx", [P, NC, NQ, COLS])
        wh = sb("wh", [P, NC, NQ, COLS])
        b_all = sb("b_all", [P, NG, 4 * U])
        bias = sb("bias", [P, 2, COLS])
        ident = sb("ident", [P, P])
        pick = sb("pick", [P, BLOCK, 2, N])
        x_rows = sb("x_rows", [ROWS, D])
        xT = sb("xT", [P, NC, ROWS])
        xproj = sb("xproj", [P, 2, COLS])
        h_rows = sb("h_rows", [P, BLOCK, NC, U])
        h0_rows = sb("h0_rows", [P, NC, U])
        hT = sb("hT", [P, NC, U])
        xy = sb("xy", [P, BLOCK, NC, U])
        gates = sb("gates", [P, 2, NC, 4 * U])
        tanh_o = sb("tanh_o", [P, NC, U])
        products = sb("products", [P, NC, 2 * U])
        tanh_c = sb("tanh_c", [P, NC, U])

        gates_ps = [[pb(f"gates_ps{k}{part}") for part in range(len(PARTS))] for k in range(2)]
        proj_ps = pb("proj_ps")
        xT_ps = pb("xT_ps")

        def c_ps(s, c):
            return gates_ps[s % 2][c][:, IFG:IFG + U]

        wx_loaded = [sem(f"wx_loaded{c}") for c in range(NC)]
        wh_loaded = sem("wh_loaded")
        b_loaded = sem("b_loaded")
        h0_loaded = sem("h0_loaded")
        x_loaded = sem("x_loaded")
        xy_loaded = sem("xy_loaded")
        y_stored = sem("y_stored")
        h0_zeroed = sem("h0_zeroed")
        zeros_set = sem("zeros_set")
        ps_zeroed = sem("ps_zeroed")
        ident_set = sem("ident_set")
        pick_set = sem("pick_set")
        wx_scaled = [sem(f"wx_scaled{c}") for c in range(NC)]
        wh_scaled = sem("wh_scaled")
        bias_set = sem("bias_set")
        h0_scaled = sem("h0_scaled")
        x_turned = sem("x_turned")
        xT_ready = sem("xT_ready")
        proj_done = sem("proj_done")
        proj_ready = sem("proj_ready")
        injected = sem("injected")
        ifg_done = [sem(f"ifg_done{c}") for c in range(NC)]
        o_done = sem("o_done")
        tanh_done = [sem(f"tanh_done{c}") for c in range(NC)]
        products_done = [sem(f"products_done{c}") for c in range(NC)]
        c_kept = sem("c_kept")
        c_ready = [sem(f"c_ready{c}") for c in range(NC)]
        tanh_c_done = [sem(f"tanh_c_done{c}") for c in range(NC)]
        h_rows_done = [sem(f"h_rows_done{c}") for c in range(NC)]
        hT_ready = [sem(f"hT_ready{c}") for c in range(NC)]
        y_ready = sem("y_ready")

        def load_wh(engine, g):
            engine.dma_start(wh_in[U * g:U * (g + 1), :, :],
                             Wh[2 * U * g:2 * U * (g + 1), :].rearrange("(c u) k -> u c k", c=NC)).then_inc(wh_loaded, 16)

        block = ctx.enter_context(nc.Block())

        @block.sync
        def _(sp):
            def load_x(k):
                sp.dma_start(x_rows[:, :], x_blocks[k]).then_inc(x_loaded, 16)

            def load_xy(k):
                for g in range(NQ):
                    sp.dma_start(xy[U * g:U * g + N, :, :, :].rearrange("p t c u -> p t (c u)"),
                                 x_quads[k, g]).then_inc(xy_loaded, 16)

            def store_y(k):
                sp.wait_ge(y_ready, 2 * k + 2)
                for g in range(NQ):
                    sp.dma_start(out_quads[k, g],
                                 xy[U * g:U * g + N, :, :, :].rearrange("p t c u -> p t (c u)")).then_inc(y_stored, 16)

            load_x(0)
            for hi in range(2):
                sp.dma_start(b_all[ROWS * hi:ROWS * (hi + 1), :, :],
                             b.rearrange("(q h j) -> h q j", q=NG, h=2)[hi].partition_broadcast(ROWS)).then_inc(b_loaded, 16)
            sp.wait_ge(h0_zeroed, 1)
            for g in range(NQ):
                sp.dma_start(h0_rows[U * g:U * g + N, :, :].rearrange("p c u -> p (c u)"),
                             cond[:, 2 * U * g:2 * U * (g + 1)]).then_inc(h0_loaded, 16)
            for g in range(NQ // 2):
                load_wh(sp, g)
            sp.wait_ge(x_turned, 1)
            load_x(1)
            sp.wait_ge(zeros_set, 2)
            load_xy(0)
            sp.wait_ge(x_turned, 2)
            load_x(2)

            def swap_xy(k):
                store_y(k)
                sp.wait_ge(y_stored, 16 * NQ * (k + 1))
                load_xy(k + 1)

            with sp.Fori(0, NBLK - 3) as k:
                swap_xy(k)
                sp.wait_ge(x_turned, k + 3)
                load_x(k + 3)
            with sp.Fori(NBLK - 3, NBLK - 1) as k:
                swap_xy(k)
            store_y(NBLK - 1)
            sp.wait_ge(y_stored, 16 * NQ * NBLK)

        @block.gpsimd
        def _(pool):
            nc.gpsimd.memset(ident[:, :], 0.0).then_inc(ident_set, 1)
            pool.wait_ge(ident_set, 1)
            nc.gpsimd.affine_select(out=ident[:, :], in_=ident[:, :], compare_op=ALU.not_equal, fill=1.0,
                                    base=0, pattern=[[-1, P]], channel_multiplier=1).then_inc(ident_set, 1)
            pool.wait_ge(ident_set, 2)
            for hi in range(2):
                nc.gpsimd.tensor_copy(pick[:, :, hi, :],
                                      ident[:, ROWS * hi:ROWS * (hi + 1)].rearrange("p (n t) -> p t n", n=N)
                                      ).then_inc(pick_set, 1)

        def gate_columns(w, q):
            a, d = GATE_AT[q], GATE_STEP[q]
            if d == U:
                return w[..., a:a + 2 * U].rearrange("... (c u) -> ... c u", c=NC)
            return w[..., 0:NC * d].rearrange("... (c d) -> ... c d", c=NC)[..., a:a + U]

        def scaled(w_out, w_in, c, q):
            return (gate_columns(w_out[:, c, :, :], q),
                    w_in[:, c, HID * q:HID * (q + 1)].rearrange("p (g c u) -> p g c u", g=NQ, c=NC))

        WX_BY_ACT = [(1, 0), (1, 1)]
        WH_BY_ACT = [(1, 0), (1, 1), (1, 2)]
        WX_SCALE = [0.5, 0.5, 0.5, 1.0]
        WH_SCALE = [0.25, 0.25, 0.25, 0.5]

        @block.scalar
        def _(act):
            for c in range(NC):
                act.dma_start(wx_in[:, c, :], Wx[P * c:P * (c + 1), :]).then_inc(wx_loaded[c], 16)
            for g in range(NQ // 2, NQ):
                load_wh(act, g)

            def copy_xT(k):
                act.wait_ge(x_turned, k + 1)
                nc.scalar.copy(xT[:, :, :], xT_ps[:, 0:NC * ROWS].rearrange("p (c r) -> p c r", c=NC)
                               ).then_inc(xT_ready, 1)

            act.wait_ge(wx_loaded[1], 16)
            for c, q in WX_BY_ACT:
                nc.scalar.mul(*scaled(wx, wx_in, c, q), WX_SCALE[q]).then_inc(wx_scaled[c], 1)
            copy_xT(1)
            act.wait_ge(wh_loaded, 16 * NQ)
            for c, q in WH_BY_ACT:
                nc.scalar.mul(*scaled(wh, wh_in, c, q), WH_SCALE[q]).then_inc(wh_scaled, 1)

            def step(k, s):
                t = BLOCK * k + s
                for c in range(NC):
                    act.wait_ge(ifg_done[c], t + 1)
                    nc.scalar.activation(gates[:, s % 2, c, 0:IFG], gates_ps[s % 2][c][:, 0:IFG],
                                         ACT.Tanh).then_inc(tanh_done[c], 1)
                act.wait_ge(o_done, t + 1)
                for c in range(NC):
                    nc.scalar.activation(tanh_o[:, c, :], gates_ps[s % 2][2][:, U * c:U * (c + 1)], ACT.Tanh)
                    act.wait_ge(c_ready[c], t + 1)
                    nc.scalar.activation(tanh_c[:, c, :], c_ps(s, c), ACT.Tanh, scale=0.5).then_inc(tanh_c_done[c], 1)

            with act.Fori(0, NBLK - 2) as k:
                for s in range(BLOCK):
                    if s == BLOCK - 1:
                        copy_xT(k + 2)
                    step(k, s)
            with act.Fori(NBLK - 2, NBLK) as k:
                for s in range(BLOCK):
                    step(k, s)

        @block.vector
        def _(dve):
            def copy_proj(k, gg):
                nc.vector.tensor_tensor(xproj[:, gg, :], proj_ps[:, COLS * gg:COLS * (gg + 1)], bias[:, gg, :],
                                        ALU.add).then_inc(proj_ready, 1)

            def add_x(k, part):
                steps_of = slice(BLOCK // 2 * part, BLOCK // 2 * (part + 1))
                xv = xy[:, steps_of, :, :].rearrange("p t c u -> p (t c u)")
                nc.vector.scalar_tensor_tensor(out=xv, in0=h_rows[:, steps_of, :, :].rearrange("p t c u -> p (t c u)"),
                                               scalar=0.5, in1=xv, op0=ALU.mult, op1=ALU.add).then_inc(y_ready, 1)

            def add_up(c, to):
                return nc.vector.scalar_tensor_tensor(out=to, in0=products[:, c, U:2 * U], scalar=0.5,
                                                      in1=products[:, c, 0:U], op0=ALU.mult, op1=ALU.add)

            def step(k, s):
                t = BLOCK * k + s

                def multiply(c):
                    G = gates[:, s % 2, c, :]
                    dve.wait_ge(tanh_done[c], t + 1)
                    nc.vector.scalar_tensor_tensor(out=products[:, c, :], in0=G[:, 0:2 * U], scalar=1.0,
                                                   in1=G[:, 2 * U:4 * U], op0=ALU.add, op1=ALU.mult
                                                   ).then_inc(products_done[c], 1)

                def new_c(c):
                    dve.wait_ge(products_done[c], t + 1)
                    add_up(c, c_ps(s, c)).then_inc(c_ready[c], 1)

                def keep_c(c):
                    add_up(c, gates[:, (s + 1) % 2, c, 3 * U:4 * U]).then_inc(c_kept, 1)

                def hidden(c):
                    dve.wait_ge(tanh_c_done[c], t + 1)
                    nc.vector.scalar_tensor_tensor(out=h_rows[:, s, c, :], in0=tanh_o[:, c, :], scalar=1.0,
                                                   in1=tanh_c[:, c, :], op0=ALU.add, op1=ALU.mult
                                                   ).then_inc(h_rows_done[c], 1)

                def turn(c):
                    dve.wait_ge(h_rows_done[c], t + 1)
                    nc.vector.transpose(hT[:, c, :], h_rows[:, s, c, :]).then_inc(hT_ready[c], 1)

                multiply(0)
                new_c(0)
                multiply(1)
                keep_c(0)
                new_c(1)
                hidden(0)
                keep_c(1)
                turn(0)
                hidden(1)
                turn(1)

            def steps(k, last=False):
                for s in range(BLOCK):
                    step(k, s)
                    if s == BLOCK // 2:
                        dve.wait_ge(xy_loaded, 16 * NQ * (k + 1))
                        add_x(k, 0)
                    if s == BLOCK - 2 and not last:
                        dve.wait_ge(proj_done, k + 2)
                        dve.wait_ge(injected, BLOCK * (k + 1))
                        copy_proj(k + 1, 0)
                        copy_proj(k + 1, 1)
                    if s == BLOCK - 1:
                        dve.wait_ge(h_rows_done[1], BLOCK * (k + 1))
                        add_x(k, 1)

            nc.vector.memset(h0_rows[:, :, :], 0.0).then_inc(h0_zeroed, 1)
            for k in range(2):
                for bank in gates_ps[k]:
                    nc.vector.memset(bank[:, 0:IFG], 0.0).then_inc(ps_zeroed, 1)
            nc.vector.memset(xy[:, :, :, :], 0.0).then_inc(zeros_set, 1)
            nc.vector.memset(gates[:, 0, :, 3 * U:4 * U], 0.0).then_inc(zeros_set, 1)
            dve.wait_ge(x_turned, 1)
            nc.vector.tensor_copy(xT[:, :, :], xT_ps[:, 0:NC * ROWS].rearrange("p (c r) -> p c r", c=NC)
                                  ).then_inc(xT_ready, 1)

            def scale_rest(w_out, w_in, c, factors, others, done):
                for q in range(NG):
                    if (c, q) not in others:
                        nc.vector.tensor_scalar(*scaled(w_out, w_in, c, q), factors[q], None, ALU.mult).then_inc(done, 1)

            for c in range(NC):
                dve.wait_ge(wx_loaded[c], 16)
                scale_rest(wx, wx_in, c, WX_SCALE, WX_BY_ACT, wx_scaled[c])
            dve.wait_ge(b_loaded, 32)
            for hi in range(2):
                part = slice(ROWS * hi, ROWS * (hi + 1))
                for q in range(NG):
                    nc.vector.tensor_scalar(gate_columns(bias[part, :, :], q),
                                            b_all[part, q, :].rearrange("p (g c u) -> p g c u", g=2, c=NC),
                                            WX_SCALE[q], None, ALU.mult).then_inc(bias_set, 1)
            dve.wait_ge(bias_set, 2 * NG)
            dve.wait_ge(proj_done, 1)
            copy_proj(0, 0)
            copy_proj(0, 1)
            dve.wait_ge(h0_loaded, 16 * NQ)
            nc.vector.tensor_scalar(h0_rows[:, :, :], h0_rows[:, :, :], 2.0, None, ALU.mult).then_inc(h0_scaled, 1)
            dve.wait_ge(h0_scaled, 1)
            for c in range(NC):
                nc.vector.transpose(hT[:, c, :], h0_rows[:, c, :]).then_inc(hT_ready[c], 1)
            dve.wait_ge(wh_loaded, 16 * NQ)
            for c in range(NC):
                scale_rest(wh, wh_in, c, WH_SCALE, WH_BY_ACT, wh_scaled)
            dve.wait_ge(zeros_set, 2)
            with dve.Fori(0, NBLK - 1) as k:
                steps(k)
            steps(NBLK - 1, last=True)

        @block.tensor
        def _(pe):
            def turn_x():
                for c in range(NC):
                    last = nc.tensor.transpose(xT_ps[:, c * ROWS:(c + 1) * ROWS], x_rows[:, c * P:(c + 1) * P],
                                               ident[0:ROWS, 0:ROWS])
                last.then_inc(x_turned, 1)

            PIECES = [(gg, at, c) for c in range(NC) for gg in range(2) for at in (0, COLS // 2)]
            assert len(PIECES) == BLOCK

            def project(piece):
                gg, at, c = PIECES[piece]
                for hi in range(2):
                    last = nc.tensor.matmul(proj_ps[ROWS * hi:ROWS * (hi + 1), COLS * gg + at:COLS * gg + at + COLS // 2],
                                            xT[:, c, :], wx[:, c, 2 * hi + gg, at:at + COLS // 2],
                                            start=(piece == 0), stop=(c == NC - 1), skip_group_check=True)
                if piece == BLOCK - 1:
                    last.then_inc(proj_done, 1)

            def bank(s, g, part, a, z):
                return gates_ps[s % 2][part][U * g:U * g + N, a:z]

            def inject(s):
                for part, cols in enumerate(PARTS):
                    for g in range(NQ):
                        last = nc.tensor.matmul(bank(s, g, part, 0, cols.stop - cols.start),
                                                pick[:, s, g // 2, :], xproj[:, g % 2, cols],
                                                start=True, stop=False, skip_group_check=True)
                last.then_inc(injected, 1)

            def recur(s, c, part, a=0, z=None):
                at = PARTS[part].start
                z = z or PARTS[part].stop - at
                for g in range(NQ):
                    last = nc.tensor.matmul(bank(s, g, part, a, z), hT[:, c, 0:N], wh[:, c, g, at + a:at + z],
                                            start=False, stop=(c == NC - 1), skip_group_check=True)
                return last

            def steps(k, ahead):
                for s in range(BLOCK):
                    t = BLOCK * k + s
                    pe.wait_ge(hT_ready[0], t + 1)
                    recur(s, 0, 0)
                    recur(s, 0, 1, 0, IFG // 2)
                    pe.wait_ge(hT_ready[1], t + 1)
                    recur(s, 1, 0).then_inc(ifg_done[0], 1)
                    recur(s, 0, 1, IFG // 2, IFG)
                    recur(s, 1, 1).then_inc(ifg_done[1], 1)
                    recur(s, 0, 2)
                    recur(s, 1, 2).then_inc(o_done, 1)
                    if s < BLOCK - 1:
                        if s == BLOCK - 2 and ahead == 2:
                            pe.wait_ge(x_loaded, 16 * (k + 3))
                        inject(s + 1)
                        if ahead:
                            project(s + 1)
                        if s == BLOCK - 2 and ahead == 2:
                            turn_x()
                    elif ahead:
                        pe.wait_ge(proj_ready, 2 * (k + 2))
                        if ahead == 2:
                            pe.wait_ge(xT_ready, k + 3)
                        inject(0)
                        if ahead == 2:
                            project(0)

            def warm_up(count):
                for _ in range(count):
                    nc.tensor.matmul(gates_ps[1][2][0:U, P:2 * P], ident[:, 0:U], ident[:, :], start=True, stop=True)

            pe.wait_ge(ident_set, 2)
            pe.wait_ge(ps_zeroed, 2 * len(PARTS))
            warm_up(7)
            pe.wait_ge(x_loaded, 16)
            turn_x()
            warm_up(6)
            pe.wait_ge(xT_ready, 1)
            for c in range(NC):
                pe.wait_ge(wx_scaled[c], NG)
                for piece in range(BLOCK // NC):
                    project(BLOCK // NC * c + piece)
            warm_up(2)
            pe.wait_ge(x_loaded, 32)
            turn_x()
            pe.wait_ge(pick_set, 2)
            pe.wait_ge(proj_ready, 2)
            inject(0)
            pe.wait_ge(xT_ready, 2)
            project(0)
            warm_up(1)
            pe.wait_ge(wh_scaled, NC * NG)
            with pe.Fori(0, NBLK - 2) as k:
                steps(k, 2)
            steps(NBLK - 2, 1)
            steps(NBLK - 1, 0)


_INS = ['x', 'cond_1024', 'L0_cond_Wx', 'L0_cond_Wh', 'L0_cond_b']
_OUTS = [((8, 256, 256), 'float32')]


def kernel(**inputs):
    import numpy as _np
    import concourse.bacc as _bacc
    from concourse import mybir as _mybir
    from concourse.bass_utils import run_bass_kernel_spmd as _run

    nc = _bacc.Bacc("TRN2", target_bir_lowering=False, num_devices=1)
    arrays, args = {}, []
    for name in _INS:
        a = _np.ascontiguousarray(inputs[name])
        arrays[f"in_{name}_dram"] = a
        args.append(nc.dram_tensor(f"in_{name}_dram", a.shape, _mybir.dt.from_np(a.dtype), kind="ExternalInput").ap())
    for i, (shape, dtype) in enumerate(_OUTS):
        dt = _mybir.dt.from_np(_np.dtype(dtype))
        args.append(nc.dram_tensor(f"out_{i}_dram", shape, dt, kind="ExternalOutput").ap())
    lstm_residual_kernel(nc, *args)
    r = _run(nc, [arrays], core_ids=[0])
    got = tuple(r.results[0][f"out_{i}_dram"] for i in range(len(_OUTS)))
    return got[0]
```
